# Optimizing a Trainium2 kernel written in Bass

```python
import numpy as np
import jax
import jax.numpy as jnp

def _softmax(x, axis=-1):
    return jax.nn.softmax(x, axis=axis)

def _gelu(x):
    return jax.nn.gelu(x, approximate=True)

def _silu(x):
    return jax.nn.silu(x)

def _sigmoid(x):
    return jax.nn.sigmoid(x)

def _layernorm(x, axis=-1, eps=1e-05):
    m = jnp.mean(x, axis=axis, keepdims=True)
    v = jnp.var(x, axis=axis, keepdims=True)
    return (x - m) / jnp.sqrt(v + eps)

def _scatter_add(tgt, idx, src, axis=0):
    return tgt.at[idx].add(src)

def _segment_sum(src, seg, n):
    return jax.ops.segment_sum(src, seg, n)
kernel_name = 'mk_rec_standalone_d1_rec_r8_f1486a'

def setup_inputs(seed: int=0):
    np.random.seed(seed)
    _w = jnp.asarray

    def _rec_inputs():
        import jax
        import jax.numpy as jnp
        _rk = jax.random.key(seed)
        r_feature = -0.0002422 + 0.999987 * jax.random.normal(jax.random.fold_in(_rk, 1), (2048, 200, 64), jnp.float32)
        return r_feature
    r_feature = _rec_inputs()

    def _L0_rec_setup():
        import jax, jax.numpy as jnp
        import numpy as np
        B, F, E = (256, 200, 64)
        key = jax.random.key(seed)
        k1, k2 = jax.random.split(key)
        feature = jax.random.normal(k1, (B, F, E), dtype=jnp.float32)
        weight = 0.01 * jax.random.normal(k2, (F, E, E), dtype=jnp.float32)
        return {'feature': feature, 'weight': weight}
    _L0_rec_all = _L0_rec_setup()
    _L0_rec_in = {k: v for k, v in _L0_rec_all.items() if k in ('weight',)}
    del _L0_rec_all
    return {'r_feature': r_feature, 'L0_rec_weight': _L0_rec_in['weight']}

def reference(r_feature, L0_rec_weight):
    import jax
    import jax.numpy as jnp

    def _L0_rec_ref(feature, weight):
        import jax, jax.numpy as jnp
        import numpy as np
        B, F, E = (256, 200, 64)
        bilinear = jnp.einsum('bie,ied->bid', feature, weight)
        out = jnp.einsum('bid,bjd->bij', bilinear, feature)
        return out
    y = _L0_rec_ref(r_feature, L0_rec_weight)
    return y

_drawn_inputs = setup_inputs


def setup_inputs(seed=0):
    import zlib

    import numpy as np

    out = dict(_drawn_inputs(seed))
    spreads = {}
    factors = {}
    for name, (base, spread) in spreads.items():
        noise = np.random.default_rng([zlib.crc32(name.encode()), seed]).standard_normal(out[name].shape)
        drawn = base * np.exp(spread * noise) if base else spread * noise
        out[name] = jnp.asarray(drawn.astype(out[name].dtype))
    for name, factor in factors.items():
        out[name] = (out[name] * factor).astype(out[name].dtype)
    return out
```

```python
from contextlib import ExitStack

import concourse.bass as bass
from concourse import mybir
from concourse.alu_op_type import AluOpType as ALU

F32 = mybir.dt.float32


def feature_interaction(nc, feature, weight, out):
    B, F, E = feature.shape
    NB = 64
    BLOCKS = B // NB
    FH = F // 2
    CF = 10
    CH = CF // 2
    CHUNKS = F // CF
    XSLOTS = 4
    PB = 2
    PAIRS = NB // PB
    GB = 2 * PB
    GROUPS = NB // GB
    OSLOTS = 4
    FA = FH // 16 * 16
    BANK = 512
    WPARTS = 4
    WF = FH // WPARTS
    assert E == 64 and CHUNKS % XSLOTS == 0 and GROUPS % OSLOTS == 0 and BLOCKS % 2 == 0
    assert WF % CH == 0 and (CH + 1) * NB <= BANK and PB * F <= BANK

    feature_v = feature.rearrange("b f e -> b (f e)")
    weight_v = weight.rearrange("(m h) e d -> h e m d", h=2)
    out_v = out.rearrange("b (m h) j -> m b (h j)", h=2)

    ctx = ExitStack()
    with ctx:
        def sbuf(name, shape):
            return ctx.enter_context(nc.sbuf_tensor(name, shape, F32))

        def psum(name, shape):
            return ctx.enter_context(nc.psum_tensor(name, shape, F32))

        def sem(name):
            return ctx.enter_context(nc.semaphore(name))

        w = sbuf("w", [128, FH + 1, E])
        ident = sbuf("ident", [128, NB])
        x = sbuf("x", [128, XSLOTS * CF + 2, E])
        ft = [sbuf(f"ft{q}", [128, NB, F + 1]) for q in range(2)]
        bl = [sbuf(f"bl{q}", [128, NB, FH]) for q in range(2)]
        staging = sbuf("staging", [FH, OSLOTS, GB, 2, F])

        ft_psum = psum("ft_psum", [128, 2, BANK])
        bl_psum = psum("bl_psum", [128, 2, BANK])
        out_psum = [psum(f"out_psum{q}", [128, 2, BANK]) for q in range(2)]

        w_loaded = [sem(f"w_loaded{i}") for i in range(WPARTS)]
        x_loaded = [sem(f"x_loaded{i}") for i in range(XSLOTS)]
        ends_zeroed = sem("ends_zeroed")
        ident_zero = sem("ident_zero")
        ident_ready = sem("ident_ready")
        transposed = sem("transposed")
        ft_stored = sem("ft_stored")
        bilinear_done = sem("bilinear_done")
        bl_stored = sem("bl_stored")
        scores_done = sem("scores_done")
        staged_even = sem("staged_even")
        staged_odd = sem("staged_odd")
        out_written = [sem(f"out_written{i}") for i in range(OSLOTS)]
        rest_written = [sem(f"rest_written{i}") for i in range(OSLOTS)]

        block = ctx.enter_context(nc.Block())

        def transposes_after(s):
            return [k for k in range(CHUNKS) if 3 * k // 2 == s]

        def bilinear_after(s):
            return [k for k in range(CHUNKS) if 3 * k // 2 + 1 == s]

        def ring_place(k):
            return 1 + CF * (k % XSLOTS)

        def steps(engine, step, last_looped=BLOCKS - 2):
            step(0, 0)
            with engine.Fori(1, last_looped, 2) as n:
                step(n, 1)
                step(n + 1, 0)
            for n in range(last_looped + 1, BLOCKS - 1):
                step(n, n % 2)

        def wait_count(engine, semaphore, count):
            if not (isinstance(count, int) and count == 0):
                engine.wait_ge(semaphore, count)

        @block.sync
        def _(sp):
            def load_x(n, q, k):
                if not isinstance(n, int) or n > 0 or k >= XSLOTS:
                    sp.wait_ge(transposed, n * CHUNKS + k - XSLOTS + (2 if k >= XSLOTS else 1))
                before = 1 if k % XSLOTS == 0 and k > 0 else 0
                sp.dma_start(x[64 * q:64 * q + NB, ring_place(k) - before:ring_place(k) + CF, :],
                             feature_v[bass.ds(n * NB, NB), E * (CF * k - before):E * CF * (k + 1)]
                             ).then_inc(x_loaded[k % XSLOTS], 16)

            def store(n, g):
                sp.wait_ge(staged_even, n * GROUPS + g + 1)
                sp.wait_ge(staged_odd, n * GROUPS + g + 1)
                sp.dma_start(out_v[0:FA, bass.ds(n * NB + GB * g, GB), :], staging[0:FA, g % OSLOTS]
                             ).then_inc(out_written[g % OSLOTS], 16)

            AHEAD = XSLOTS - 1

            def step(n, q):
                for s in range(PAIRS):
                    for k in transposes_after(s):
                        if k + AHEAD < CHUNKS:
                            load_x(n + 1, 1 - q, k + AHEAD)
                        elif not (isinstance(n, int) and n == BLOCKS - 2):
                            load_x(n + 2, q, k + AHEAD - CHUNKS)
                    if s % 2 == 1 and s >= 3:
                        store(n, (s - 3) // 2)
                store(n, GROUPS - 1)

            load_x(0, 0, 0)
            for part in range(WPARTS):
                for h in range(2):
                    sp.dma_start(w[64 * h:64 * h + 64, WF * part + h:WF * (part + 1) + h, :],
                                 weight_v[h, :, WF * part:WF * (part + 1), :]
                                 ).then_inc(w_loaded[part], 16)
                load_x(0, 0, part + 1)
            for k in range(WPARTS + 1, CHUNKS):
                load_x(0, 0, k)
            for k in range(AHEAD):
                load_x(1, 1, k)
            steps(sp, step, BLOCKS - 4)
            for g in range(GROUPS):
                store(BLOCKS - 1, g)
            for slot in range(OSLOTS):
                sp.wait_ge(out_written[slot], 16 * BLOCKS * GROUPS // OSLOTS)
                sp.wait_ge(rest_written[slot], 16 * BLOCKS * GROUPS // OSLOTS)

        @block.gpsimd
        def _(pool):
            nc.gpsimd.memset(ident[:], 0.0).then_inc(ident_zero, 1)
            for h in range(2):
                pool.wait_ge(ident_zero, h + 1)
                nc.gpsimd.affine_select(out=ident[:], in_=ident[:], compare_op=ALU.not_equal, fill=1.0,
                                        base=-64 * h, pattern=[[-1, NB]], channel_multiplier=1
                                        ).then_inc(ident_ready if h else ident_zero, 1)

            def store_rest(n, g):
                pool.wait_ge(staged_even, n * GROUPS + g + 1)
                pool.wait_ge(staged_odd, n * GROUPS + g + 1)
                pool.dma_start(out_v[FA:FH, bass.ds(n * NB + GB * g, GB), :], staging[FA:FH, g % OSLOTS]
                               ).then_inc(rest_written[g % OSLOTS], 16)

            with pool.Fori(0, BLOCKS) as n:
                for g in range(GROUPS):
                    store_rest(n, g)

        @block.tensor
        def _(pe):
            def transposes(n, q, k):
                pe.wait_ge(x_loaded[k % XSLOTS], 16 * (n * (CHUNKS // XSLOTS) + k // XSLOTS + 1))
                wait_count(pe, ft_stored, n * CHUNKS + k)
                pe.nop(nofuse=True)
                pe.wait_ge(ident_ready, 1)
                for c in range(CF + (k == CHUNKS - 1)):
                    place = ring_place(k) + c - 1
                    bank, col = min(c // CH, 1), c - CH * min(c // CH, 1)
                    last = nc.tensor.transpose(ft_psum[:, bank, NB * col:NB * (col + 1)],
                                               x[64 * q:64 * q + NB, place:place + 2, :],
                                               ident[64 * q:64 * q + NB, :])
                last.then_inc(transposed, 1)

            def bilinear(n, q, k):
                pe.wait_ge(ft_stored, n * CHUNKS + k + 1)
                wait_count(pe, bl_stored, n * CHUNKS + k)
                if isinstance(n, int) and n == 0 and CH * k % WF == 0:
                    pe.wait_ge(w_loaded[CH * k // WF], 32)
                for c in range(CH):
                    m = CH * k + c
                    for h in range(2):
                        last = nc.tensor.matmul(bl_psum[:, h, NB * c:NB * (c + 1)],
                                                w[64 * h:64 * h + 64, m:m + 2, :],
                                                ft[q][64 * h:64 * h + 64, :, 2 * m + 1],
                                                start=True, stop=True)
                last.then_inc(bilinear_done, 1)

            def scores(n, q, s):
                if s == 0:
                    pe.wait_ge(bl_stored, n * CHUNKS + CHUNKS)
                wait_count(pe, staged_odd if s % 2 else staged_even, n * (PAIRS // 2) + s // 2)
                for b in range(PB):
                    for h in range(2):
                        last = nc.tensor.matmul(out_psum[s % 2][0:FH, h, F * b:F * (b + 1)],
                                                bl[q][64 * h:64 * h + 64, PB * s + b, :],
                                                ft[q][64 * h:64 * h + 64, PB * s + b, 1 - h:1 - h + F],
                                                start=True, stop=True)
                last.then_inc(scores_done, 1)

            def step(n, q):
                for s in range(PAIRS):
                    scores(n, q, s)
                    for k in transposes_after(s):
                        transposes(n + 1, 1 - q, k)
                    for k in bilinear_after(s):
                        bilinear(n + 1, 1 - q, k)

            pe.wait_ge(ends_zeroed, 1)
            transposes(0, 0, 0)
            for k in range(1, CHUNKS):
                transposes(0, 0, k)
                bilinear(0, 0, k - 1)
            bilinear(0, 0, CHUNKS - 1)
            steps(pe, step)
            for s in range(PAIRS):
                scores(BLOCKS - 1, 1, s)

        def stage_pair(engine, copy, staged, n, s):
            g = s // 2
            engine.wait_ge(scores_done, n * PAIRS + s + 1)
            uses = n * (GROUPS // OSLOTS) + g // OSLOTS
            wait_count(engine, out_written[g % OSLOTS], 16 * uses)
            wait_count(engine, rest_written[g % OSLOTS], 16 * uses)
            b = PB * (s % 2)
            copy(staging[:, g % OSLOTS, b:b + PB, :, :].rearrange("p b h j -> p h b j"),
                 out_psum[s % 2][0:FH, :, 0:PB * F].rearrange("p h (b j) -> p h b j", j=F)
                 ).then_inc(staged, 1)

        @block.vector
        def _(dve):
            def store_ft(n, q, k):
                dve.wait_ge(transposed, n * CHUNKS + k + 1)
                if k == CHUNKS - 1:
                    nc.vector.tensor_copy(ft[q][:, :, F], ft_psum[:, 1, CH * NB:(CH + 1) * NB])
                nc.vector.tensor_copy(
                    ft[q][:, :, CF * k:CF * (k + 1)].rearrange("p b (g c) -> p g b c", g=2),
                    ft_psum[:, :, 0:CH * NB].rearrange("p g (c b) -> p g b c", b=NB)
                    ).then_inc(ft_stored, 1)

            def step(n, q):
                for s in range(PAIRS):
                    if s % 2 == 0:
                        stage_pair(dve, nc.vector.tensor_copy, staged_even, n, s)
                    for k in transposes_after(s):
                        store_ft(n + 1, 1 - q, k)

            nc.vector.memset(x[:, 0, :], 0.0)
            nc.vector.memset(x[:, XSLOTS * CF + 1, :], 0.0)
            nc.vector.memset(w[0:64, FH, :], 0.0)
            nc.vector.memset(w[64:128, 0, :], 0.0).then_inc(ends_zeroed, 1)
            for k in range(CHUNKS):
                store_ft(0, 0, k)
            steps(dve, step)
            for s in range(0, PAIRS, 2):
                stage_pair(dve, nc.vector.tensor_copy, staged_even, BLOCKS - 1, s)

        @block.scalar
        def _(act):
            def store_bl(n, q, k):
                act.wait_ge(bilinear_done, n * CHUNKS + k + 1)
                for h in range(2):
                    last = nc.scalar.copy(bl[q][64 * h:64 * h + 64, :, CH * k:CH * (k + 1)],
                                          bl_psum[64 * h:64 * h + 64, h, 0:CH * NB].rearrange(
                                              "p (c b) -> p b c", b=NB))
                last.then_inc(bl_stored, 1)

            def step(n, q):
                for s in range(PAIRS):
                    if s % 2 == 1:
                        stage_pair(act, nc.scalar.copy, staged_odd, n, s)
                    for k in bilinear_after(s):
                        store_bl(n + 1, 1 - q, k)

            for k in range(CHUNKS):
                store_bl(0, 0, k)
            steps(act, step)
            for s in range(1, PAIRS, 2):
                stage_pair(act, nc.scalar.copy, staged_odd, BLOCKS - 1, s)


def kernel(r_feature, L0_rec_weight):
    import numpy as np
    import concourse.bacc as bacc
    from concourse.bass_utils import run_bass_kernel_spmd

    nc = bacc.Bacc("TRN2", target_bir_lowering=False, num_devices=1, dynamic_dma_scratch_size=4096)
    feature = np.ascontiguousarray(r_feature)
    weight = np.ascontiguousarray(L0_rec_weight)
    B, F, _ = feature.shape
    feature_dram = nc.dram_tensor("feature_dram", feature.shape, F32, kind="ExternalInput").ap()
    weight_dram = nc.dram_tensor("weight_dram", weight.shape, F32, kind="ExternalInput").ap()
    out_dram = nc.dram_tensor("out_dram", (B, F, F), F32, kind="ExternalOutput").ap()
    feature_interaction(nc, feature_dram, weight_dram, out_dram)
    done = run_bass_kernel_spmd(nc, [{"feature_dram": feature, "weight_dram": weight}], core_ids=[0])
    return done.results[0]["out_dram"]
```

```python
from contextlib import ExitStack

import concourse.bass as bass
from concourse import mybir
from concourse.alu_op_type import AluOpType as ALU

F32 = mybir.dt.float32


def feature_interaction(nc, feature, weight, out):
    B, F, E = feature.shape
    NB = 128
    BLOCKS = B // NB
    FH = F // 2
    BANK = 512
    WB = BANK // NB
    CF = 2 * WB
    CHUNKS = F // CF
    COPIES = CHUNKS + 1
    XSLOTS = 3
    PB = 2
    PAIRS = NB // PB
    SETS = 4
    BL_SET = 2
    OSLOTS = 5
    FA = FH // 16 * 16
    WPARTS = 4
    WF = FH // WPARTS
    assert 2 * E == 128 and F % CF == 0 and B % NB == 0 and FH % WPARTS == 0
    assert PB * F <= BANK and PAIRS % SETS == 0 and CHUNKS % 2 == 1

    feature_v = feature.rearrange("b f e -> b (f e)")
    weight_v = weight.rearrange("(m h) e d -> h e m d", h=2)
    out_v = out.rearrange("b (m h) j -> m b (h j)", h=2)

    ctx = ExitStack()
    with ctx:
        def sbuf(name, shape):
            return ctx.enter_context(nc.sbuf_tensor(name, shape, F32))

        def sem(name):
            return ctx.enter_context(nc.semaphore(name))

        w = sbuf("w", [128, FH, 128])
        ident = sbuf("ident", [128, 128])
        x = sbuf("x", [128, 1 + XSLOTS * CF, E])
        ft = sbuf("ft", [128, NB, F + 1])
        bl = sbuf("bl", [128, NB, FH])
        staging = sbuf("staging", [FH, OSLOTS, PB, 2, F])
        ps = [ctx.enter_context(nc.psum_tensor(f"ps{q}", [128, 2, BANK], F32)) for q in range(SETS)]

        w_zeroed = sem("w_zeroed")
        w_loaded = [sem(f"w_loaded{i}") for i in range(WPARTS)]
        x_loaded = [sem(f"x_loaded{i}") for i in range(XSLOTS)]
        x_zeroed = sem("x_zeroed")
        ident_zero = sem("ident_zero")
        ident_ready = sem("ident_ready")
        transposed = sem("transposed")
        ft_low = sem("ft_low")
        ft_high = sem("ft_high")
        bilinear_done = sem("bilinear_done")
        bl_stored = sem("bl_stored")
        scores_done = sem("scores_done")
        staged_even = sem("staged_even")
        staged_odd = sem("staged_odd")
        out_written = [sem(f"out_written{i}") for i in range(OSLOTS)]

        block = ctx.enter_context(nc.Block())

        def uses(total, slots, slot):
            return (total - slot + slots - 1) // slots

        def blocks(engine, body):
            body(0)
            with engine.Fori(1, BLOCKS) as n:
                body(n)

        def wait_count(engine, semaphore, count):
            if not (isinstance(count, int) and count == 0):
                engine.wait_ge(semaphore, count)

        @block.sync
        def _(sp):
            def load_x(n, k):
                slot = k % XSLOTS
                if k >= XSLOTS:
                    sp.wait_ge(transposed, n * COPIES + k - XSLOTS + 2)
                elif not isinstance(n, int):
                    sp.wait_ge(transposed, n * COPIES)
                before = 1 if slot == 0 and k > 0 else 0
                place = 1 + CF * slot
                sp.dma_start(x[:, place - before:place + CF, :],
                             feature_v[bass.ds(n * NB, NB), E * (CF * k - before):E * CF * (k + 1)]
                             ).then_inc(x_loaded[slot], 16)

            def store(n, s):
                sp.wait_ge(staged_odd if s % 2 else staged_even, n * (PAIRS // 2) + s // 2 + 1)
                for a, b in ((0, FA), (FA, FH)):
                    sp.dma_start(out_v[a:b, bass.ds(n * NB + PB * s, PB), :], staging[a:b, s % OSLOTS]
                                 ).then_inc(out_written[s % OSLOTS], 16)

            def body(n, last=False):
                for k in range(XSLOTS, CHUNKS):
                    load_x(n, k)
                if not last:
                    for k in range(XSLOTS):
                        load_x(n + 1, k)
                for s in range(PAIRS):
                    store(n, s)

            for k in range(XSLOTS):
                load_x(0, k)
            for part in range(WPARTS):
                for h in range(2):
                    sp.dma_start(w[64 * h:64 * h + 64, WF * part:WF * (part + 1), 64 * h:64 * h + 64],
                                 weight_v[h, :, WF * part:WF * (part + 1), :]
                                 ).then_inc(w_loaded[part], 16)
            with sp.Fori(0, BLOCKS - 1) as n:
                body(n)
            body(BLOCKS - 1, last=True)
            for slot in range(OSLOTS):
                sp.wait_ge(out_written[slot], 32 * BLOCKS * uses(PAIRS, OSLOTS, slot))

        @block.gpsimd
        def _(pool):
            nc.gpsimd.memset(ident[:], 0.0).then_inc(ident_zero, 1)
            pool.wait_ge(ident_zero, 1)
            nc.gpsimd.affine_select(out=ident[:], in_=ident[:], compare_op=ALU.not_equal, fill=1.0,
                                    base=0, pattern=[[-1, 128]], channel_multiplier=1
                                    ).then_inc(ident_ready, 1)
            pool.wait_ge(ident_ready, 1)
            for part in range(WPARTS):
                for h in range(2):
                    if part + h:
                        pool.wait_ge(w_zeroed, 2 * part + h)
                    nc.gpsimd.memset(w[64 * h:64 * h + 64, WF * part:WF * (part + 1),
                                       64 * (1 - h):64 * (1 - h) + 64], 0.0).then_inc(w_zeroed, 1)

        @block.tensor
        def _(pe):
            def transposes(n, k):
                if k < CHUNKS:
                    pe.wait_ge(x_loaded[k % XSLOTS],
                               16 * (n * uses(CHUNKS, XSLOTS, k % XSLOTS) + k // XSLOTS + 1))
                if k >= 2:
                    pe.wait_ge(ft_low, n * COPIES + k - 1)
                    pe.wait_ge(ft_high, n * CHUNKS + k - 1)
                else:
                    wait_count(pe, staged_odd if k else staged_even, n * (PAIRS // 2))
                for c in range(CF if k < CHUNKS else 1):
                    place = CF * (k % XSLOTS) + c
                    if k == CHUNKS:
                        place = CF * ((k - 1) % XSLOTS + 1)
                    last = nc.tensor.transpose(ps[k % 2][:, c // WB, NB * (c % WB):NB * (c % WB + 1)],
                                               x[:, place:place + 2, :], ident[:])
                last.then_inc(transposed, 1)

            def bilinear(n, k):
                pe.wait_ge(ft_low, n * COPIES + k + 1)
                pe.wait_ge(ft_high, n * CHUNKS + k + 1)
                if k >= 2:
                    pe.wait_ge(bl_stored, n * CHUNKS + k - 1)
                elif k == 0:
                    wait_count(pe, staged_odd if BL_SET % 2 else staged_even, n * (PAIRS // 2))
                for c in range(WB):
                    m = WB * k + c
                    if isinstance(n, int) and n == 0 and m % WF == 0:
                        pe.wait_ge(w_loaded[m // WF], 32)
                        pe.wait_ge(w_zeroed, 2 * (m // WF + 1))
                    last = nc.tensor.matmul(ps[BL_SET][:, k % 2, NB * c:NB * (c + 1)], w[:, m, :],
                                            ft[:, :, 2 * m + 1], start=True, stop=True)
                last.then_inc(bilinear_done, 1)

            def scores(n, s):
                if s == 0:
                    pe.wait_ge(ft_low, (n + 1) * COPIES)
                    pe.wait_ge(bl_stored, (n + 1) * CHUNKS)
                if s >= SETS:
                    pe.wait_ge(staged_odd if s % 2 else staged_even,
                               n * (PAIRS // 2) + (s - SETS) // 2 + 1)
                elif s == SETS - 1:
                    wait_count(pe, staged_odd if s % 2 else staged_even, n * (PAIRS // 2))
                for b in range(PB):
                    for h in range(2):
                        last = nc.tensor.matmul(ps[s % SETS][0:FH, h, F * b:F * (b + 1)],
                                                bl[64 * h:64 * h + 64, PB * s + b, :],
                                                ft[64 * h:64 * h + 64, PB * s + b, 1 - h:1 - h + F],
                                                start=True, stop=True)
                last.then_inc(scores_done, 1)

            def body(n):
                transposes(n, 0)
                for k in range(CHUNKS):
                    transposes(n, k + 1)
                    bilinear(n, k)
                for s in range(PAIRS):
                    scores(n, s)

            pe.wait_ge(ident_ready, 1)
            pe.wait_ge(x_zeroed, 1)
            blocks(pe, body)

        def copy_to_ft(engine, copy, stored, n, k, bank):
            engine.wait_ge(transposed, n * COPIES + k + 1)
            windows = WB if k < CHUNKS else 1
            at = CF * k + WB * bank
            copy(ft[:, :, at:at + windows],
                 ps[k % 2][:, bank, 0:NB * windows].rearrange("p (c b) -> p b c", b=NB)
                 ).then_inc(stored, 1)

        def stage_pair(engine, copy, staged, n, s):
            slot = s % OSLOTS
            engine.wait_ge(scores_done, n * PAIRS + s + 1)
            wait_count(engine, out_written[slot], 32 * (n * uses(PAIRS, OSLOTS, slot) + s // OSLOTS))
            copy(staging[:, slot, :, :, :].rearrange("p b h j -> p h b j"),
                 ps[s % SETS][0:FH, :, 0:PB * F].rearrange("p h (b j) -> p h b j", j=F)
                 ).then_inc(staged, 1)

        @block.vector
        def _(dve):
            def body(n):
                for k in range(COPIES):
                    copy_to_ft(dve, nc.vector.tensor_copy, ft_low, n, k, 0)
                for s in range(0, PAIRS, 2):
                    stage_pair(dve, nc.vector.tensor_copy, staged_even, n, s)

            nc.vector.memset(x[:, 0, :], 0.0).then_inc(x_zeroed, 1)
            blocks(dve, body)

        @block.scalar
        def _(act):
            def copy_to_bl(n, k):
                act.wait_ge(bilinear_done, n * CHUNKS + k + 1)
                nc.scalar.copy(bl[:, :, WB * k:WB * (k + 1)],
                               ps[BL_SET][:, k % 2, :].rearrange("p (c b) -> p b c", b=NB)
                               ).then_inc(bl_stored, 1)

            def body(n):
                copy_to_ft(act, nc.scalar.copy, ft_high, n, 0, 1)
                for k in range(1, CHUNKS):
                    copy_to_ft(act, nc.scalar.copy, ft_high, n, k, 1)
                    copy_to_bl(n, k - 1)
                copy_to_bl(n, CHUNKS - 1)
                for s in range(1, PAIRS, 2):
                    stage_pair(act, nc.scalar.copy, staged_odd, n, s)

            blocks(act, body)


def kernel(r_feature, L0_rec_weight):
    import numpy as np
    import concourse.bacc as bacc
    from concourse.bass_utils import run_bass_kernel_spmd

    nc = bacc.Bacc("TRN2", target_bir_lowering=False, num_devices=1, dynamic_dma_scratch_size=512)
    feature = np.ascontiguousarray(r_feature)
    weight = np.ascontiguousarray(L0_rec_weight)
    B, F, _ = feature.shape
    feature_dram = nc.dram_tensor("feature_dram", feature.shape, F32, kind="ExternalInput").ap()
    weight_dram = nc.dram_tensor("weight_dram", weight.shape, F32, kind="ExternalInput").ap()
    out_dram = nc.dram_tensor("out_dram", (B, F, F), F32, kind="ExternalOutput").ap()
    feature_interaction(nc, feature_dram, weight_dram, out_dram)
    done = run_bass_kernel_spmd(nc, [{"feature_dram": feature, "weight_dram": weight}], core_ids=[0])
    return done.results[0]["out_dram"]
```

```python
from contextlib import ExitStack

import concourse.bass as bass
from concourse import mybir
from concourse.alu_op_type import AluOpType as ALU

F32 = mybir.dt.float32


def feature_interaction(nc, feature, weight, out):
    B, F, E = feature.shape
    NB = 128
    BLOCKS = B // NB
    FH = F // 2
    BANK = 512
    WB = BANK // NB
    CF = 2 * WB
    CHUNKS = F // CF
    AHEAD = 2
    XSLOTS = 5
    PB = 2
    PAIRS = NB // PB
    SETS = 3
    OSLOTS = 4
    FA = FH // 16 * 16
    WPARTS = 10
    WF = FH // WPARTS
    assert 2 * E == 128 and F % CF == 0 and B % NB == 0 and FH % WPARTS == 0
    assert PB * F <= BANK and PAIRS % OSLOTS == 0 and PAIRS % SETS == 1 and CHUNKS % 4 == 1
    assert CHUNKS % XSLOTS == 0 and OSLOTS % 2 == 0

    feature_v = feature.rearrange("b f e -> b (f e)")
    weight_v = weight.rearrange("(m h) e d -> h e m d", h=2)
    out_v = out.rearrange("b (m h) j -> m b (h j)", h=2)

    ctx = ExitStack()
    with ctx:
        def sbuf(name, shape):
            return ctx.enter_context(nc.sbuf_tensor(name, shape, F32))

        def sem(name):
            return ctx.enter_context(nc.semaphore(name))

        w = sbuf("w", [128, FH, 128])
        ident = sbuf("ident", [128, 128])
        x = sbuf("x", [128, XSLOTS, CF * E])
        ft = sbuf("ft", [128, NB, F + 1])
        bl = sbuf("bl", [128, NB, FH])
        staging = sbuf("staging", [FH, OSLOTS, PB, 2, F])
        ps = [ctx.enter_context(nc.psum_tensor(f"ps{q}", [128, 2, BANK], F32)) for q in range(4)]
        transpose_bank = [ps[3][:, 0, :], ps[3][:, 1, :], ps[2][:, 0, :], ps[2][:, 1, :]]
        bilinear_bank = [ps[1][:, 0, :], ps[1][:, 1, :]]

        w_zeroed = sem("w_zeroed")
        w_loaded = [sem(f"w_loaded{i}") for i in range(WPARTS)]
        x_loaded = [sem(f"x_loaded{i}") for i in range(XSLOTS)]
        ident_zero = sem("ident_zero")
        ident_ready = sem("ident_ready")
        transposed = sem("transposed")
        in_place = [sem("in_place_even"), sem("in_place_odd")]
        swapped = [sem("swapped_even"), sem("swapped_odd")]
        bilinear_done = sem("bilinear_done")
        bl_stored = [sem("bl_stored_even"), sem("bl_stored_odd")]
        scores_done = sem("scores_done")
        staged = [sem("staged_even"), sem("staged_odd")]
        out_written = [sem(f"out_written{i}") for i in range(OSLOTS)]
        rest_written = [sem(f"rest_written{i}") for i in range(OSLOTS // 2)]

        block = ctx.enter_context(nc.Block())

        def of_parity(total, q):
            return (total + 1 - q) // 2

        def chunks_done(n, k):
            return n * of_parity(CHUNKS, k % 2) + k // 2 + 1

        def pairs_done(n, s):
            return n * (PAIRS // 2) + s // 2 + 1

        def blocks(engine, body):
            body(0)
            with engine.Fori(1, BLOCKS - 1) as n:
                body(n)
            body(BLOCKS - 1)

        def has_next(n):
            return not (isinstance(n, int) and n == BLOCKS - 1)

        def starts(n):
            return isinstance(n, int) and n == 0

        @block.sync
        def _(sp):
            def load_x(n, k):
                slot = k % XSLOTS
                if not (starts(n) and k < XSLOTS):
                    sp.wait_ge(transposed, n * CHUNKS + k - XSLOTS + 1)
                sp.dma_start(x[:, slot, :],
                             feature_v[bass.ds(n * NB, NB), E * CF * k:E * CF * (k + 1)]
                             ).then_inc(x_loaded[slot], 16)

            def load_w(part):
                for h in range(2):
                    sp.dma_start(w[64 * h:64 * h + 64, WF * part:WF * (part + 1), 64 * h:64 * h + 64],
                                 weight_v[h, :, WF * part:WF * (part + 1), :]
                                 ).then_inc(w_loaded[part], 16)

            def store(n, s):
                sp.wait_ge(staged[s % 2], pairs_done(n, s))
                slot = s % OSLOTS
                sp.dma_start(out_v[0:FA, bass.ds(n * NB + PB * s, PB), :], staging[0:FA, slot]
                             ).then_inc(out_written[slot], 16)
                if s % 2:
                    sp.dma_start(out_v[FA:FH, bass.ds(n * NB + PB * (s - 1), 2 * PB), :],
                                 staging[FA:FH, slot - 1:slot + 1].rearrange("p s b h j -> p (s b) (h j)")
                                 ).then_inc(rest_written[slot // 2], 16)

            def body(n):
                for k in range(XSLOTS + AHEAD, CHUNKS):
                    if starts(n) and k in w_with_chunk:
                        load_w(w_with_chunk[k])
                    load_x(n, k)
                if has_next(n):
                    for k in range(XSLOTS):
                        load_x(n + 1, k)
                for s in range(PAIRS):
                    store(n, s)
                    if s == PAIRS // 8 and has_next(n):
                        for k in range(XSLOTS, XSLOTS + AHEAD):
                            load_x(n + 1, k)

            first = XSLOTS + AHEAD
            w_with_chunk = {WF * part // WB: part for part in range((first + 1) // 2, WPARTS)}
            assert min(w_with_chunk) >= first
            for k in range(first):
                load_x(0, k)
                if k % 2 == 0:
                    load_w(k // 2)
            blocks(sp, body)
            for slot in range(OSLOTS):
                sp.wait_ge(out_written[slot], 16 * BLOCKS * PAIRS // OSLOTS)
                if slot % 2:
                    sp.wait_ge(rest_written[slot // 2], 16 * BLOCKS * PAIRS // OSLOTS)

        @block.gpsimd
        def _(pool):
            nc.gpsimd.memset(ident[:], 0.0).then_inc(ident_zero, 1)
            pool.wait_ge(ident_zero, 1)
            nc.gpsimd.affine_select(out=ident[:], in_=ident[:], compare_op=ALU.not_equal, fill=1.0,
                                    base=0, pattern=[[-1, 128]], channel_multiplier=1
                                    ).then_inc(ident_ready, 1)
            pool.wait_ge(ident_ready, 1)
            for part in range(WPARTS):
                for h in range(2):
                    if part + h:
                        pool.wait_ge(w_zeroed, 2 * part + h)
                    nc.gpsimd.memset(w[64 * h:64 * h + 64, WF * part:WF * (part + 1),
                                       64 * (1 - h):64 * (1 - h) + 64], 0.0).then_inc(w_zeroed, 1)

        @block.tensor
        def _(pe):
            def transposes(n, k):
                slot = k % XSLOTS
                pe.wait_ge(x_loaded[slot], 16 * (n * (CHUNKS // XSLOTS) + k // XSLOTS + 1))
                if k >= 4:
                    pe.wait_ge(swapped[k % 2], chunks_done(n, k - 4))
                elif k < AHEAD:
                    if not starts(n):
                        pe.wait_ge(swapped[k % 2], chunks_done(n - 1, CHUNKS - 1 - 3 * k))
                elif not starts(n):
                    pe.wait_ge(staged[(PAIRS - 2) % 2], pairs_done(n - 1, PAIRS - 2))
                for c in range(WB):
                    last = nc.tensor.transpose(transpose_bank[k % 4][:, NB * c:NB * (c + 1)],
                                               x[:, slot, 2 * E * c:2 * E * (c + 1)], ident[:])
                last.then_inc(transposed, 1)

            def bilinear(n, k):
                pe.wait_ge(in_place[k % 2], chunks_done(n, k))
                if k >= 2:
                    pe.wait_ge(bl_stored[k % 2], chunks_done(n, k - 2))
                elif not starts(n):
                    pe.wait_ge(staged[(PAIRS - 3) % 2], pairs_done(n - 1, PAIRS - 3))
                for c in range(WB):
                    m = WB * k + c
                    if starts(n) and m % WF == 0:
                        pe.wait_ge(w_loaded[m // WF], 32)
                        pe.wait_ge(w_zeroed, 2 * (m // WF + 1))
                    last = nc.tensor.matmul(bilinear_bank[k % 2][:, NB * c:NB * (c + 1)], w[:, m, :],
                                            ft[:, :, 2 * m + 1], start=True, stop=True)
                last.then_inc(bilinear_done, 1)

            def scores(n, s):
                if s == 0:
                    for k in (CHUNKS - 2, CHUNKS - 1):
                        pe.wait_ge(swapped[k % 2], chunks_done(n, k))
                        pe.wait_ge(bl_stored[k % 2], chunks_done(n, k))
                    if not starts(n):
                        pe.wait_ge(staged[(PAIRS - 1) % 2], pairs_done(n - 1, PAIRS - 1))
                if s >= SETS:
                    pe.wait_ge(staged[(s - SETS) % 2], pairs_done(n, s - SETS))
                for b in range(PB):
                    for h in range(2):
                        last = nc.tensor.matmul(ps[s % SETS][0:FH, h, F * b:F * (b + 1)],
                                                bl[64 * h:64 * h + 64, PB * s + b, :],
                                                ft[64 * h:64 * h + 64, PB * s + b, 1 - h:1 - h + F],
                                                start=True, stop=True)
                last.then_inc(scores_done, 1)

            def body(n):
                transposes(n, AHEAD)
                transposes(n, AHEAD + 1)
                for k in range(CHUNKS):
                    if k >= 2 and k + AHEAD < CHUNKS:
                        transposes(n, k + AHEAD)
                    bilinear(n, k)
                if has_next(n):
                    for k in range(AHEAD):
                        transposes(n + 1, k)
                for s in range(PAIRS):
                    scores(n, s)

            pe.wait_ge(ident_ready, 1)
            for k in range(AHEAD):
                transposes(0, k)
            blocks(pe, body)

        def copy_in_place(engine, copy, n, k):
            engine.wait_ge(transposed, n * CHUNKS + k + 1)
            if k < AHEAD and not starts(n):
                engine.wait_ge(scores_done, n * PAIRS)
            pairs = transpose_bank[k % 4].rearrange("p (c b) -> p b c", b=NB)
            copy(ft[:, :, CF * k + 1:CF * (k + 1):2], pairs).then_inc(in_place[k % 2], 1)

        def copy_swapped(copy, k):
            pairs = transpose_bank[k % 4].rearrange("p (c b) -> p b c", b=NB)
            copy(ft[64:128, :, CF * k:CF * (k + 1):2], pairs[0:64])
            copy(ft[0:64, :, CF * k + 2:CF * (k + 1) + 1:2], pairs[64:128]).then_inc(swapped[k % 2], 1)

        def copy_to_bl(engine, copy, n, k):
            engine.wait_ge(bilinear_done, n * CHUNKS + k + 1)
            copy(bl[:, :, WB * k:WB * (k + 1)],
                 bilinear_bank[k % 2].rearrange("p (c b) -> p b c", b=NB)).then_inc(bl_stored[k % 2], 1)

        def stage_pair(engine, copy, n, s):
            slot = s % OSLOTS
            engine.wait_ge(scores_done, n * PAIRS + s + 1)
            if s >= OSLOTS or not starts(n):
                engine.wait_ge(out_written[slot], 16 * (n * (PAIRS // OSLOTS) + s // OSLOTS))
                engine.wait_ge(rest_written[slot // 2], 16 * (n * (PAIRS // OSLOTS) + s // OSLOTS))
            copy(staging[:, slot, :, :, :].rearrange("p b h j -> p h b j"),
                 ps[s % SETS][0:FH, :, 0:PB * F].rearrange("p h (b j) -> p h b j", j=F)
                 ).then_inc(staged[s % 2], 1)

        def copies(engine, copy, n, q):
            for k in range(q, CHUNKS, 2):
                copy_in_place(engine, copy, n, k)
                if k >= 2:
                    copy_to_bl(engine, copy, n, k - 2)
                copy_swapped(copy, k)
            copy_to_bl(engine, copy, n, k)
            for s in range(q, PAIRS, 2):
                stage_pair(engine, copy, n, s)

        @block.vector
        def _(dve):
            blocks(dve, lambda n: copies(dve, nc.vector.tensor_copy, n, 1))

        @block.scalar
        def _(act):
            blocks(act, lambda n: copies(act, nc.scalar.copy, n, 0))


def kernel(r_feature, L0_rec_weight):
    import numpy as np
    import concourse.bacc as bacc
    from concourse.bass_utils import run_bass_kernel_spmd

    nc = bacc.Bacc("TRN2", target_bir_lowering=False, num_devices=1, dynamic_dma_scratch_size=256)
    feature = np.ascontiguousarray(r_feature)
    weight = np.ascontiguousarray(L0_rec_weight)
    B, F, _ = feature.shape
    feature_dram = nc.dram_tensor("feature_dram", feature.shape, F32, kind="ExternalInput").ap()
    weight_dram = nc.dram_tensor("weight_dram", weight.shape, F32, kind="ExternalInput").ap()
    out_dram = nc.dram_tensor("out_dram", (B, F, F), F32, kind="ExternalOutput").ap()
    feature_interaction(nc, feature_dram, weight_dram, out_dram)
    done = run_bass_kernel_spmd(nc, [{"feature_dram": feature, "weight_dram": weight}], core_ids=[0])
    return done.results[0]["out_dram"]
```
